# Optimizing a Trainium2 kernel written in Bass

```python
import numpy as np
import jax
import jax.numpy as jnp

def _softmax(x, axis=-1):
    return jax.nn.softmax(x, axis=axis)

def _gelu(x):
    return jax.nn.gelu(x, approximate=True)

def _silu(x):
    return jax.nn.silu(x)

def _sigmoid(x):
    return jax.nn.sigmoid(x)

def _layernorm(x, axis=-1, eps=1e-05):
    m = jnp.mean(x, axis=axis, keepdims=True)
    v = jnp.var(x, axis=axis, keepdims=True)
    return (x - m) / jnp.sqrt(v + eps)

def _scatter_add(tgt, idx, src, axis=0):
    return tgt.at[idx].add(src)

def _segment_sum(src, seg, n):
    return jax.ops.segment_sum(src, seg, n)
kernel_name = 'mk_adj_preln_d1_adj_r2_ef0f2d'

def setup_inputs(seed: int=0):
    np.random.seed(seed)
    _w = jnp.asarray

    def _rec_inputs():
        import jax
        import jax.numpy as jnp
        _gk = jax.random.key(seed)
        x = -0.0005207 + 1.001 * jax.random.normal(jax.random.fold_in(_gk, 1), (8192, 128), jnp.float32)
        _w = (1.0 + jnp.arange(8192, dtype=jnp.float32)) ** (-0.5)
        _w = _w / _w.mean()
        _pij = jnp.clip(0.000244141 * _w[:, None] * _w[None, :], 0.0, 1.0)
        _a = jax.random.uniform(jax.random.fold_in(_gk, 2), (8192, 8192)) < _pij
        _a = jnp.logical_or(_a, jnp.eye(8192, dtype=bool))
        _af = _a.astype(jnp.float32)
        _af = _af * jax.random.uniform(jax.random.fold_in(_gk, 3), (8192, 8192), jnp.float32, 0.05, 1)
        adj = _af
        return (x, adj)
    x, adj = _rec_inputs()

    def _L0_gnn_setup():
        import jax, jax.numpy as jnp
        import numpy as np
        ALPHA = 0.1
        N, F = (8192, 128)
        key = jax.random.key(seed)
        k1, k2, k3 = jax.random.split(key, 3)
        x = jax.random.normal(k1, (N, F), dtype=jnp.float32)
        adj = jax.random.uniform(k2, (N, N), dtype=jnp.float32)
        h = jax.random.normal(k3, (N, F), dtype=jnp.float32)
        return {'x': x, 'adj': adj, 'h': h}
    _L0_gnn_all = _L0_gnn_setup()
    _L0_gnn_in = {k: v for k, v in _L0_gnn_all.items() if k in ('h',)}
    del _L0_gnn_all
    return {'x': x, 'adj': adj, 'L0_gnn_h': _L0_gnn_in['h']}

def reference(x, adj, L0_gnn_h):
    import jax
    import jax.numpy as jnp

    def _L0_gnn_ref(x, adj, h):
        import jax, jax.numpy as jnp
        import numpy as np
        ALPHA = 0.1
        N, F = (8192, 128)
        return (1.0 - ALPHA) * (adj @ x) + ALPHA * h
    h = jnp.maximum(_layernorm(x, axis=-1), 0.0)
    x = x + _L0_gnn_ref(h, adj, L0_gnn_h)
    return x

_drawn_inputs = setup_inputs


def setup_inputs(seed=0):
    import zlib

    import numpy as np

    out = dict(_drawn_inputs(seed))
    spreads = {}
    factors = {}
    for name, (base, spread) in spreads.items():
        noise = np.random.default_rng([zlib.crc32(name.encode()), seed]).standard_normal(out[name].shape)
        drawn = base * np.exp(spread * noise) if base else spread * noise
        out[name] = jnp.asarray(drawn.astype(out[name].dtype))
    for name, factor in factors.items():
        out[name] = (out[name] * factor).astype(out[name].dtype)
    return out
```

```python
from contextlib import ExitStack

import concourse.bass as bass
from concourse import mybir

F32 = mybir.dt.float32
F32R = mybir.dt.float32r
ALU = mybir.AluOpType
ACT = mybir.ActivationFunctionType

ALPHA = 0.1
EPS = 1e-05
P = 128
BM = 512
TILES_U = 4
SPLIT = (3, 2)
TILES_G = TILES_U * len(SPLIT)
SPLIT_G = sum(SPLIT)
RING = 8
SLOTS = 2
HALF = 4096.0
BELOW = 1.0 - 2.0 ** -13


def gnn_layer(nc, x_rows, adj_t, x_t, h_t, out_t):
    F = x_rows.shape[2]
    KT = x_rows.shape[1]
    BLOCKS, UNITS = adj_t.shape[0], adj_t.shape[1]
    GROUPS = KT // TILES_G
    LAPS = UNITS // RING
    assert F == P and UNITS * TILES_U == KT and UNITS % RING == 0 and UNITS % len(SPLIT) == 0
    NSPLIT = [SPLIT[u % len(SPLIT)] for u in range(UNITS)]
    PART0 = [sum(NSPLIT[:u]) for u in range(UNITS)]

    with ExitStack() as ctx:
        def sb(name, shape, dt=F32):
            return ctx.enter_context(nc.sbuf_tensor(name, shape, dt))

        def sem(name):
            return ctx.enter_context(nc.semaphore(name))

        h_sb = sb("h_sb", [P, KT, F])
        h1_sb = sb("h1_sb", [P, sum(NSPLIT), F], F32R)
        h2_sb = sb("h2_sb", [P, sum(NSPLIT), F], F32R)
        e_sb = sb("e_sb", [P, sum(NSPLIT), F], F32R)
        adj_sb = sb("adj_sb", [P, RING, TILES_U, BM])
        a1_sb = sb("a1_sb", [P, SLOTS, max(SPLIT), BM], F32R)
        a2_sb = sb("a2_sb", [P, SLOTS, max(SPLIT), BM], F32R)
        d_sb = sb("d_sb", [P, SLOTS, max(SPLIT), BM], F32R)
        xt_sb = sb("xt_sb", [P, BM])
        ht_sb = sb("ht_sb", [P, BM])
        small_sb = sb("small_sb", [P, BM])
        out_sb = sb("out_sb", [P, BM])
        stats = sb("stats", [P, TILES_G, 6])
        mean2 = sb("mean2", [P, TILES_G])
        mean = sb("mean", [P, TILES_G])
        gap = sb("gap", [P, TILES_G])
        gap2 = sb("gap2", [P, TILES_G])
        spread = sb("spread", [P, TILES_G])
        within = sb("within", [P, TILES_G])
        var = sb("var", [P, TILES_G])
        std = sb("std", [P, TILES_G])
        rstd = sb("rstd", [P, TILES_G])
        large = ctx.enter_context(nc.psum_tensor("large", [P, BM], F32))
        small = ctx.enter_context(nc.psum_tensor("small", [P, BM], F32))

        x_loaded = sem("x_loaded")
        adj_loaded = [sem(f"adj_loaded{j}") for j in range(RING)]
        base_loaded = sem("base_loaded")
        unit_used = sem("unit_used")
        ln_step = sem("ln_step")
        var_ready = sem("var_ready")
        std_ready = sem("std_ready")
        rstd_ready = sem("rstd_ready")
        h_ready = sem("h_ready")
        h1_ready = sem("h1_ready")
        e_ready = sem("e_ready")
        h_split = sem("h_split")
        a1_ready = sem("a1_ready")
        a2_ready = sem("a2_ready")
        d_ready = sem("d_ready")
        a1_free = sem("a1_free")
        parts_free = sem("parts_free")
        small_ready = sem("small_ready")
        small_copied = sem("small_copied")
        large_copied = sem("large_copied")
        base_summed = sem("base_summed")
        partly_summed = sem("partly_summed")
        out_ready = sem("out_ready")
        stored = sem("stored")

        block = ctx.enter_context(nc.Block())

        @block.sync
        def _(sp):
            def load_x(g):
                sp.dma_start(h_sb[:, g * TILES_G:(g + 1) * TILES_G, :],
                             x_rows[:, g * TILES_G:(g + 1) * TILES_G, :]).then_inc(x_loaded, 16)

            def load_unit(i, u):
                sp.dma_start(adj_sb[:, u % RING, :, :], adj_t[i, u]).then_inc(adj_loaded[u % RING], 16)

            def load_base(i):
                sp.dma_start(xt_sb[:, :], x_t[i]).then_inc(base_loaded, 16)
                sp.dma_start(ht_sb[:, :], h_t[i]).then_inc(base_loaded, 16)

            per = UNITS // GROUPS
            load_x(0)
            for u in range(UNITS):
                if u >= RING:
                    sp.wait_ge(unit_used, u - RING + 1)
                load_unit(0, u)
                if u % per == 0 and u // per + 1 < GROUPS:
                    sp.wait_ge(x_loaded, 16 * (u // per + 1))
                    load_x(u // per + 1)
            load_base(0)
            with sp.Fori(1, BLOCKS) as i:
                for u in range(UNITS):
                    sp.wait_ge(unit_used, i * UNITS + (u - RING + 1))
                    load_unit(i, u)
                    if u == RING + 4:
                        sp.wait_ge(out_ready, i)
                        load_base(i)

        @block.tensor
        def _(pe):
            def plain(u, k, first, last):
                mm = nc.tensor.matmul(large[:, :], h_sb[:, u * TILES_U + k, :], adj_sb[:, u % RING, k, :],
                                      start=first, stop=last)
                return mm

            for u in range(UNITS):
                if u % (UNITS // GROUPS) == 0:
                    pe.wait_ge(h_ready, u // (UNITS // GROUPS) + 1)
                pe.wait_ge(adj_loaded[u % RING], 16 * (u // RING + 1))
                for k in range(TILES_U):
                    mm = plain(u, k, u == 0 and k == 0, u == UNITS - 1 and k == TILES_U - 1)
                mm.then_inc(unit_used, 1)

            pe.wait_ge(h_split, GROUPS)
            with pe.Fori(1, BLOCKS) as i:
                for u in range(UNITS):
                    s, n = u % SLOTS, NSPLIT[u]
                    unit = (i - 1) * UNITS + (u + 1)
                    if u == 0:
                        pe.wait_ge(small_copied, i)
                    pe.wait_ge(a1_ready, unit)
                    for k in range(n):
                        nc.tensor.matmul(small[:, :], h1_sb[:, PART0[u] + k, :], a1_sb[:, s, k, :],
                                         start=(u == 0 and k == 0), stop=False)
                    pe.wait_ge(a2_ready, unit)
                    for k in range(n):
                        mm = nc.tensor.matmul(small[:, :], h2_sb[:, PART0[u] + k, :], a2_sb[:, s, k, :],
                                              start=False, stop=(u == UNITS - 1 and k == n - 1))
                    if u == UNITS - 1:
                        mm.then_inc(small_ready, 1)
                    if u == 0:
                        pe.wait_ge(large_copied, i)
                    pe.wait_ge(d_ready, unit)
                    for k in range(n):
                        mm = nc.tensor.matmul(large[:, :], e_sb[:, PART0[u] + k, :], d_sb[:, s, k, :],
                                              start=(u == 0 and k == 0), stop=False)
                        if k == 0:
                            mm.then_inc(a1_free, 1)
                    mm.then_inc(parts_free, 1)
                    pe.wait_ge(adj_loaded[u % RING], i * (16 * LAPS) + 16 * (u // RING + 1))
                    for k in range(n, TILES_U):
                        mm = plain(u, k, False, u == UNITS - 1 and k == TILES_U - 1)
                    mm.then_inc(unit_used, 1)

        @block.scalar
        def _(act):
            with act.Fori(0, GROUPS) as g:
                act.wait_ge(var_ready, g + 1)
                nc.scalar.activation(std[:, :], var[:, :], ACT.Sqrt).then_inc(std_ready, 1)
                act.wait_ge(rstd_ready, g + 1)
                for k in range(TILES_G):
                    tile = h_sb[:, bass.ds(g * TILES_G + k, 1), :]
                    last = nc.scalar.activation(tile, tile, ACT.Copy, scale=rstd[:, k:k + 1])
                last.then_inc(h_ready, 1)
                act.wait_ge(h_ready, g + 1)
                for j, n in enumerate(SPLIT):
                    last = nc.scalar.activation(h1_sb[:, bass.ds(g * SPLIT_G + sum(SPLIT[:j]), n), :],
                                                h_sb[:, bass.ds(g * TILES_G + j * TILES_U, n), :],
                                                ACT.Copy, scale=BELOW / HALF)
                last.then_inc(h1_ready, 1)
                act.wait_ge(e_ready, g + 1)
                part = e_sb[:, bass.ds(g * SPLIT_G, SPLIT_G), :]
                nc.scalar.activation(part, part.bitcast(F32), ACT.Copy, scale=HALF).then_inc(h_split, 1)

            def copy_small(i):
                act.wait_ge(small_ready, i)
                nc.scalar.activation(small_sb[:, :], small[:, :], ACT.Copy,
                                     scale=(1.0 - ALPHA) * (HALF + 1.0)).then_inc(small_copied, 1)

            def copy_large(i):
                act.wait_ge(unit_used, i * UNITS)
                nc.scalar.activation(out_sb[:, :], large[:, :], ACT.Copy,
                                     scale=1.0 - ALPHA).then_inc(large_copied, 1)

            def store(i):
                act.wait_ge(out_ready, i)
                act.dma_start(out_t[i - 1], out_sb[:, :]).then_inc(stored, 16)

            with act.Fori(1, BLOCKS) as i:
                for u in range(UNITS):
                    s, n = u % SLOTS, NSPLIT[u]
                    act.wait_ge(adj_loaded[u % RING], i * (16 * LAPS) + 16 * (u // RING + 1))
                    act.wait_ge(a1_free, i * UNITS + (u - UNITS + 1))
                    nc.scalar.activation(a1_sb[:, s, 0:n, :], adj_sb[:, u % RING, 0:n, :],
                                         ACT.Copy, scale=BELOW).then_inc(a1_ready, 1)
                    if u == 0:
                        copy_small(i)
                    if u == 1:
                        copy_large(i)
                    if u == 8:
                        store(i)
                    if u == UNITS - 1:
                        act.wait_ge(stored, i * 16)
            copy_small(BLOCKS)
            copy_large(BLOCKS)
            store(BLOCKS)
            act.wait_ge(stored, 16 * BLOCKS)

        @block.vector
        def _(dve):
            dve.sem_inc(a1_free, SLOTS)
            dve.sem_inc(parts_free, SLOTS)
            nc.vector.memset(small[:, :], 0.0).then_inc(small_ready, 1)

            with dve.Fori(0, GROUPS) as g:
                STEPS = 3
                dve.wait_ge(x_loaded, g * 16 + 16)
                for k in range(TILES_G):
                    last = nc.vector.bn_stats(stats[:, k, :], h_sb[:, bass.ds(g * TILES_G + k, 1), :])
                last.then_inc(ln_step, 1)
                dve.wait_ge(ln_step, g * STEPS + 1)
                nc.vector.tensor_tensor(mean2[:, :], stats[:, :, 1], stats[:, :, 4], ALU.add)
                nc.vector.tensor_tensor(gap[:, :], stats[:, :, 1], stats[:, :, 4], ALU.subtract)
                nc.vector.tensor_tensor(spread[:, :], stats[:, :, 2], stats[:, :, 5],
                                        ALU.add).then_inc(ln_step, 1)
                dve.wait_ge(ln_step, g * STEPS + 2)
                nc.vector.tensor_scalar(mean[:, :], mean2[:, :], 0.5, None, ALU.mult)
                nc.vector.tensor_scalar(within[:, :], spread[:, :], 1.0 / F, EPS, ALU.mult, ALU.add)
                nc.vector.scalar_tensor_tensor(gap2[:, :], gap[:, :], 0.25, gap[:, :],
                                               ALU.mult, ALU.mult).then_inc(ln_step, 1)
                dve.wait_ge(ln_step, g * STEPS + 3)
                nc.vector.tensor_tensor(var[:, :], within[:, :], gap2[:, :], ALU.add).then_inc(var_ready, 1)
                for k in range(TILES_G):
                    tile = h_sb[:, bass.ds(g * TILES_G + k, 1), :]
                    nc.vector.tensor_scalar(tile, tile, mean[:, k:k + 1], 0.0, ALU.subtract, ALU.max)
                dve.wait_ge(std_ready, g + 1)
                nc.vector.reciprocal(rstd[:, :], std[:, :]).then_inc(rstd_ready, 1)
                dve.wait_ge(h1_ready, g + 1)
                for j, n in enumerate(SPLIT):
                    part = bass.ds(g * SPLIT_G + sum(SPLIT[:j]), n)
                    h = h_sb[:, bass.ds(g * TILES_G + j * TILES_U, n), :]
                    h1 = h1_sb[:, part, :].bitcast(F32)
                    nc.vector.scalar_tensor_tensor(h2_sb[:, part, :], h1, -HALF, h, ALU.mult, ALU.add)
                    last = nc.vector.scalar_tensor_tensor(e_sb[:, part, :], h1, -(HALF + 1.0), h,
                                                          ALU.mult, ALU.add)
                last.then_inc(e_ready, 1)

            def base(i):
                dve.wait_ge(base_loaded, i * 32 + 32)
                nc.vector.scalar_tensor_tensor(xt_sb[:, :], ht_sb[:, :], ALPHA, xt_sb[:, :],
                                               ALU.mult, ALU.add).then_inc(base_summed, 1)

            def finish(i):
                dve.wait_ge(base_summed, i)
                dve.wait_ge(small_copied, i)
                nc.vector.tensor_tensor(xt_sb[:, :], xt_sb[:, :], small_sb[:, :],
                                        ALU.add).then_inc(partly_summed, 1)
                dve.wait_ge(partly_summed, i)
                dve.wait_ge(large_copied, i)
                nc.vector.tensor_tensor(out_sb[:, :], out_sb[:, :], xt_sb[:, :],
                                        ALU.add).then_inc(out_ready, 1)

            base(0)
            with dve.Fori(1, BLOCKS) as i:
                for u in range(UNITS):
                    s, n = u % SLOTS, NSPLIT[u]
                    unit = i * UNITS + (u - UNITS + 1)
                    a = adj_sb[:, u % RING, 0:n, :]
                    a1 = a1_sb[:, s, 0:n, :].bitcast(F32)
                    dve.wait_ge(a1_ready, unit)
                    dve.wait_ge(parts_free, unit)
                    nc.vector.tensor_tensor(a2_sb[:, s, 0:n, :], a, a1, ALU.subtract).then_inc(a2_ready, 1)
                    nc.vector.scalar_tensor_tensor(d_sb[:, s, 0:n, :], a1, 1.0 + 1.0 / HALF, a,
                                                   ALU.mult, ALU.subtract).then_inc(d_ready, 1)
                    if u == 2:
                        finish(i)
                    if u == 12:
                        base(i)
            finish(BLOCKS)


def kernel(x, adj, L0_gnn_h):
    import numpy as np
    import concourse.bacc as bacc
    from concourse.bass_utils import run_bass_kernel_spmd

    x, adj, h = (np.asarray(a) for a in (x, adj, L0_gnn_h))
    N, F = x.shape
    blocks, units = N // BM, N // (P * TILES_U)

    def transposed_blocks(a):
        return np.ascontiguousarray(a.reshape(blocks, BM, F).transpose(0, 2, 1))

    arrays = {
        "x_rows": np.ascontiguousarray(x.reshape(N // P, P, F).transpose(1, 0, 2)),
        "adj_t": np.ascontiguousarray(adj.reshape(blocks, BM, units, TILES_U, P).transpose(0, 2, 4, 3, 1)),
        "x_t": transposed_blocks(x),
        "h_t": transposed_blocks(h),
    }
    nc = bacc.Bacc("TRN2", target_bir_lowering=False, num_devices=1)
    args = [nc.dram_tensor(name, a.shape, F32, kind="ExternalInput").ap() for name, a in arrays.items()]
    out = nc.dram_tensor("out_t", (blocks, F, BM), F32, kind="ExternalOutput").ap()
    gnn_layer(nc, *args, out)
    r = run_bass_kernel_spmd(nc, [arrays], core_ids=[0])
    return np.ascontiguousarray(r.results[0]["out_t"].transpose(0, 2, 1).reshape(N, F))
```

```python
from contextlib import ExitStack

import concourse.bass as bass
from concourse import mybir

F32 = mybir.dt.float32
F32R = mybir.dt.float32r
ALU = mybir.AluOpType
ACT = mybir.ActivationFunctionType

ALPHA = 0.1
EPS = 1e-05
P = 128
BM = 512
TILES_U = 4
SPLIT = (3, 2)
TILES_G = TILES_U * len(SPLIT)
SPLIT_G = sum(SPLIT)
FIRST = 10
LAST = 14
RING = 8
SLOTS = 2
HALF = 4096.0
BELOW = 1.0 - 2.0 ** -13


def gnn_layer(nc, x_rows, adj_t, x_t, h_t, out_t):
    F = x_rows.shape[2]
    KT = x_rows.shape[1]
    BLOCKS, UNITS = adj_t.shape[0], adj_t.shape[1]
    GROUPS = KT // TILES_G
    LAPS = UNITS // RING
    assert F == P and UNITS * TILES_U == KT and UNITS % RING == 0 and UNITS % len(SPLIT) == 0
    NSPLIT = [SPLIT[u % len(SPLIT)] for u in range(UNITS)]
    PART0 = [sum(NSPLIT[:u]) for u in range(UNITS)]
    assert FIRST % SLOTS == 0

    def split_units(i, u):
        return i * UNITS + (u - FIRST)

    with ExitStack() as ctx:
        def sb(name, shape, dt=F32):
            return ctx.enter_context(nc.sbuf_tensor(name, shape, dt))

        def sem(name):
            return ctx.enter_context(nc.semaphore(name))

        h_sb = sb("h_sb", [P, KT, F])
        h1_sb = sb("h1_sb", [P, sum(NSPLIT), F], F32R)
        h2_sb = sb("h2_sb", [P, sum(NSPLIT), F], F32R)
        e_sb = sb("e_sb", [P, sum(NSPLIT), F], F32R)
        adj_sb = sb("adj_sb", [P, RING, TILES_U, BM])
        a1_sb = sb("a1_sb", [P, SLOTS, max(SPLIT), BM], F32R)
        a2_sb = sb("a2_sb", [P, SLOTS, max(SPLIT), BM], F32R)
        d_sb = sb("d_sb", [P, SLOTS, max(SPLIT), BM], F32R)
        xt_sb = sb("xt_sb", [P, BM])
        ht_sb = sb("ht_sb", [P, BM])
        small_sb = sb("small_sb", [P, BM])
        out_sb = sb("out_sb", [P, BM])
        stats = sb("stats", [P, TILES_G, 6])
        mean2 = sb("mean2", [P, TILES_G])
        shift = sb("shift", [P, TILES_G])
        gap = sb("gap", [P, TILES_G])
        gap2 = sb("gap2", [P, TILES_G])
        spread = sb("spread", [P, TILES_G])
        within = sb("within", [P, TILES_G])
        var = sb("var", [P, TILES_G])
        std = sb("std", [P, TILES_G])
        rough = sb("rough", [P, TILES_G])
        square = sb("square", [P, TILES_G])
        error = sb("error", [P, TILES_G])
        rstd = sb("rstd", [P, TILES_G])
        large = ctx.enter_context(nc.psum_tensor("large", [P, BM], F32))
        small = ctx.enter_context(nc.psum_tensor("small", [P, BM], F32))

        x_loaded = sem("x_loaded")
        adj_loaded = [sem(f"adj_loaded{j}") for j in range(RING)]
        base_loaded = sem("base_loaded")
        unit_used = sem("unit_used")
        ln_step = sem("ln_step")
        var_ready = sem("var_ready")
        std_ready = sem("std_ready")
        rstd_ready = sem("rstd_ready")
        scale_ready = sem("scale_ready")
        h_ready = sem("h_ready")
        h1_ready = sem("h1_ready")
        e_ready = sem("e_ready")
        h_split = sem("h_split")
        a1_ready = sem("a1_ready")
        a2_ready = sem("a2_ready")
        d_ready = sem("d_ready")
        a1_free = sem("a1_free")
        parts_free = sem("parts_free")
        small_ready = sem("small_ready")
        small_copied = sem("small_copied")
        large_copied = sem("large_copied")
        base_summed = sem("base_summed")
        partly_summed = sem("partly_summed")
        out_ready = sem("out_ready")
        stored = sem("stored")

        block = ctx.enter_context(nc.Block())

        @block.sync
        def _(sp):
            def load_x(g):
                sp.dma_start(h_sb[:, g * TILES_G:(g + 1) * TILES_G, :],
                             x_rows[:, g * TILES_G:(g + 1) * TILES_G, :]).then_inc(x_loaded, 16)

            def load_unit(i, u):
                sp.dma_start(adj_sb[:, u % RING, :, :], adj_t[i, u]).then_inc(adj_loaded[u % RING], 16)

            def load_base(i):
                sp.dma_start(xt_sb[:, :], x_t[i]).then_inc(base_loaded, 16)
                sp.dma_start(ht_sb[:, :], h_t[i]).then_inc(base_loaded, 16)

            load_x(0)
            for u in range(UNITS):
                if u >= RING:
                    sp.wait_ge(unit_used, u - RING + 1)
                load_unit(0, u)
                if u + 1 < GROUPS:
                    sp.wait_ge(x_loaded, 16 * (u + 1))
                    load_x(u + 1)
            load_base(0)
            with sp.Fori(1, BLOCKS) as i:
                for u in range(UNITS):
                    sp.wait_ge(unit_used, i * UNITS + (u - RING + 1))
                    load_unit(i, u)
                    if u == RING + 4:
                        sp.wait_ge(out_ready, i)
                        load_base(i)

        @block.tensor
        def _(pe):
            def split_products(i, u, first, last):
                s, n, count = u % SLOTS, NSPLIT[u], split_units(i, u) + 1
                if first and not isinstance(i, int):
                    pe.wait_ge(small_copied, i)
                pe.wait_ge(a1_ready, count)
                for k in range(n):
                    nc.tensor.matmul(small[:, :], h1_sb[:, PART0[u] + k, :], a1_sb[:, s, k, :],
                                     start=(first and k == 0), stop=False)
                pe.wait_ge(a2_ready, count)
                for k in range(n):
                    mm = nc.tensor.matmul(small[:, :], h2_sb[:, PART0[u] + k, :], a2_sb[:, s, k, :],
                                          start=False, stop=(last and k == n - 1))
                if last:
                    mm.then_inc(small_ready, 1)
                if first and not isinstance(i, int):
                    pe.wait_ge(large_copied, i)
                pe.wait_ge(d_ready, count)
                for k in range(n):
                    mm = nc.tensor.matmul(large[:, :], e_sb[:, PART0[u] + k, :], d_sb[:, s, k, :],
                                          start=(u == 0 and k == 0), stop=False)
                    if k == 0:
                        mm.then_inc(a1_free, 1)
                mm.then_inc(parts_free, 1)

            def plain_products(i, u, k0):
                pe.wait_ge(adj_loaded[u % RING], i * (16 * LAPS) + 16 * (u // RING + 1))
                for k in range(k0, TILES_U):
                    mm = nc.tensor.matmul(large[:, :], h_sb[:, u * TILES_U + k, :], adj_sb[:, u % RING, k, :],
                                          start=(u == 0 and k == 0), stop=(u == UNITS - 1 and k == TILES_U - 1))
                mm.then_inc(unit_used, 1)

            for u in range(UNITS):
                if u % len(SPLIT) == 0:
                    pe.wait_ge(h_ready, u // len(SPLIT) + 1)
                if u >= FIRST:
                    if u % len(SPLIT) == 0 or u == FIRST:
                        pe.wait_ge(h_split, u // len(SPLIT) + 1)
                    split_products(0, u, u == FIRST, u == UNITS - 1)
                plain_products(0, u, NSPLIT[u] if u >= FIRST else 0)
            with pe.Fori(1, BLOCKS - 1) as i:
                for u in range(UNITS):
                    split_products(i, u, u == 0, u == UNITS - 1)
                    plain_products(i, u, NSPLIT[u])
            pe.wait_ge(small_copied, BLOCKS - 1)
            pe.wait_ge(large_copied, BLOCKS - 1)
            for u in range(UNITS):
                if u < LAST:
                    split_products(BLOCKS - 1, u, u == 0, u == LAST - 1)
                plain_products(BLOCKS - 1, u, NSPLIT[u] if u < LAST else 0)

        @block.scalar
        def _(act):
            def deviation(g):
                act.wait_ge(var_ready, g + 1)
                nc.scalar.activation(std[:, :], var[:, :], ACT.Sqrt).then_inc(std_ready, 1)

            def normalise(g):
                act.wait_ge(scale_ready, g + 1)
                for k in range(TILES_G):
                    tile = h_sb[:, bass.ds(g * TILES_G + k, 1), :]
                    last = nc.scalar.activation(tile, tile, ACT.Relu, scale=rstd[:, k:k + 1],
                                                bias=shift[:, k:k + 1])
                last.then_inc(h_ready, 1)

            def leading_h(g):
                act.wait_ge(h_ready, g + 1)
                for j, n in enumerate(SPLIT):
                    last = nc.scalar.activation(h1_sb[:, bass.ds(g * SPLIT_G + sum(SPLIT[:j]), n), :],
                                                h_sb[:, bass.ds(g * TILES_G + j * TILES_U, n), :],
                                                ACT.Copy, scale=BELOW / HALF)
                last.then_inc(h1_ready, 1)

            def scale_e(g):
                act.wait_ge(e_ready, g + 1)
                part = e_sb[:, bass.ds(g * SPLIT_G, SPLIT_G), :]
                nc.scalar.activation(part, part.bitcast(F32), ACT.Copy, scale=HALF).then_inc(h_split, 1)

            deviation(0)
            normalise(0)
            with act.Fori(1, GROUPS) as g:
                deviation(g)
                leading_h(g - 1)
                normalise(g)
                scale_e(g - 1)
            leading_h(GROUPS - 1)
            scale_e(GROUPS - 1)

            def copy_small(i):
                act.wait_ge(small_ready, i)
                nc.scalar.activation(small_sb[:, :], small[:, :], ACT.Copy,
                                     scale=(1.0 - ALPHA) * (HALF + 1.0)).then_inc(small_copied, 1)

            def copy_large(i):
                act.wait_ge(unit_used, i * UNITS)
                nc.scalar.activation(out_sb[:, :], large[:, :], ACT.Copy,
                                     scale=1.0 - ALPHA).then_inc(large_copied, 1)

            def store(i):
                act.wait_ge(out_ready, i)
                act.dma_start(out_t[i - 1], out_sb[:, :]).then_inc(stored, 16)

            def leading_part(i, u):
                s, n = u % SLOTS, NSPLIT[u]
                act.wait_ge(adj_loaded[u % RING], i * (16 * LAPS) + 16 * (u // RING + 1))
                act.wait_ge(a1_free, split_units(i, u) + 1)
                nc.scalar.activation(a1_sb[:, s, 0:n, :], adj_sb[:, u % RING, 0:n, :],
                                     ACT.Copy, scale=BELOW).then_inc(a1_ready, 1)

            def rest(i, u):
                if u == 0:
                    copy_small(i)
                if u == 1:
                    copy_large(i)
                if u == 8:
                    store(i)
                if u == UNITS - 1:
                    act.wait_ge(stored, i * 16)

            for u in range(FIRST, UNITS):
                leading_part(0, u)
            with act.Fori(1, BLOCKS - 1) as i:
                for u in range(UNITS):
                    leading_part(i, u)
                    rest(i, u)
            for u in range(UNITS):
                if u < LAST:
                    leading_part(BLOCKS - 1, u)
                rest(BLOCKS - 1, u)
            copy_small(BLOCKS)
            copy_large(BLOCKS)
            store(BLOCKS)
            act.wait_ge(stored, 16 * BLOCKS)

        @block.vector
        def _(dve):
            dve.sem_inc(a1_free, SLOTS)
            dve.sem_inc(parts_free, SLOTS)

            def normalisation(g):
                STEPS = 6
                dve.wait_ge(x_loaded, g * 16 + 16)
                for k in range(TILES_G):
                    last = nc.vector.bn_stats(stats[:, k, :], h_sb[:, bass.ds(g * TILES_G + k, 1), :])
                last.then_inc(ln_step, 1)
                dve.wait_ge(ln_step, g * STEPS + 1)
                nc.vector.tensor_tensor(gap[:, :], stats[:, :, 1], stats[:, :, 4], ALU.subtract)
                nc.vector.tensor_tensor(spread[:, :], stats[:, :, 2], stats[:, :, 5], ALU.add)
                nc.vector.tensor_tensor(mean2[:, :], stats[:, :, 1], stats[:, :, 4],
                                        ALU.add).then_inc(ln_step, 1)
                dve.wait_ge(ln_step, g * STEPS + 2)
                nc.vector.tensor_scalar(within[:, :], spread[:, :], 1.0 / F, EPS, ALU.mult, ALU.add)
                nc.vector.scalar_tensor_tensor(gap2[:, :], gap[:, :], 0.25, gap[:, :],
                                               ALU.mult, ALU.mult).then_inc(ln_step, 1)
                dve.wait_ge(ln_step, g * STEPS + 3)
                nc.vector.tensor_tensor(var[:, :], within[:, :], gap2[:, :], ALU.add).then_inc(var_ready, 1)
                dve.wait_ge(std_ready, g + 1)
                nc.vector.reciprocal(rough[:, :], std[:, :]).then_inc(ln_step, 1)
                dve.wait_ge(ln_step, g * STEPS + 4)
                nc.vector.tensor_tensor(square[:, :], rough[:, :], rough[:, :], ALU.mult).then_inc(ln_step, 1)
                dve.wait_ge(ln_step, g * STEPS + 5)
                nc.vector.scalar_tensor_tensor(error[:, :], square[:, :], -0.5, var[:, :],
                                               ALU.mult, ALU.mult).then_inc(ln_step, 1)
                dve.wait_ge(ln_step, g * STEPS + 6)
                if not isinstance(g, int):
                    dve.wait_ge(h_ready, g)
                nc.vector.scalar_tensor_tensor(rstd[:, :], error[:, :], 1.5, rough[:, :],
                                               ALU.add, ALU.mult).then_inc(rstd_ready, 1)
                dve.wait_ge(rstd_ready, g + 1)
                nc.vector.scalar_tensor_tensor(shift[:, :], mean2[:, :], -0.5, rstd[:, :],
                                               ALU.mult, ALU.mult).then_inc(scale_ready, 1)

            def trailing_h(g):
                dve.wait_ge(h1_ready, g + 1)
                for j, n in enumerate(SPLIT):
                    part = bass.ds(g * SPLIT_G + sum(SPLIT[:j]), n)
                    h = h_sb[:, bass.ds(g * TILES_G + j * TILES_U, n), :]
                    h1 = h1_sb[:, part, :].bitcast(F32)
                    nc.vector.scalar_tensor_tensor(h2_sb[:, part, :], h1, -HALF, h, ALU.mult, ALU.add)
                    last = nc.vector.scalar_tensor_tensor(e_sb[:, part, :], h1, -(HALF + 1.0), h,
                                                          ALU.mult, ALU.add)
                last.then_inc(e_ready, 1)

            normalisation(0)
            with dve.Fori(1, GROUPS) as g:
                normalisation(g)
                trailing_h(g - 1)
            trailing_h(GROUPS - 1)

            def base(i):
                dve.wait_ge(base_loaded, i * 32 + 32)
                nc.vector.scalar_tensor_tensor(xt_sb[:, :], ht_sb[:, :], ALPHA, xt_sb[:, :],
                                               ALU.mult, ALU.add).then_inc(base_summed, 1)

            def finish(i):
                dve.wait_ge(base_summed, i)
                dve.wait_ge(small_copied, i)
                nc.vector.tensor_tensor(xt_sb[:, :], xt_sb[:, :], small_sb[:, :],
                                        ALU.add).then_inc(partly_summed, 1)
                dve.wait_ge(partly_summed, i)
                dve.wait_ge(large_copied, i)
                nc.vector.tensor_tensor(out_sb[:, :], out_sb[:, :], xt_sb[:, :],
                                        ALU.add).then_inc(out_ready, 1)

            def trailing_parts(i, u):
                s, n, count = u % SLOTS, NSPLIT[u], split_units(i, u) + 1
                a = adj_sb[:, u % RING, 0:n, :]
                a1 = a1_sb[:, s, 0:n, :].bitcast(F32)
                dve.wait_ge(a1_ready, count)
                dve.wait_ge(parts_free, count)
                nc.vector.tensor_tensor(a2_sb[:, s, 0:n, :], a, a1, ALU.subtract).then_inc(a2_ready, 1)
                nc.vector.scalar_tensor_tensor(d_sb[:, s, 0:n, :], a1, 1.0 + 1.0 / HALF, a,
                                               ALU.mult, ALU.subtract).then_inc(d_ready, 1)

            for u in range(FIRST, UNITS):
                trailing_parts(0, u)
            base(0)
            with dve.Fori(1, BLOCKS - 1) as i:
                for u in range(UNITS):
                    trailing_parts(i, u)
                    if u == 2:
                        finish(i)
                    if u == 12:
                        base(i)
            for u in range(LAST):
                trailing_parts(BLOCKS - 1, u)
                if u == 2:
                    finish(BLOCKS - 1)
                if u == 12:
                    base(BLOCKS - 1)
            finish(BLOCKS)


def kernel(x, adj, L0_gnn_h):
    import numpy as np
    import concourse.bacc as bacc
    from concourse.bass_utils import run_bass_kernel_spmd

    x, adj, h = (np.asarray(a) for a in (x, adj, L0_gnn_h))
    N, F = x.shape
    blocks, units = N // BM, N // (P * TILES_U)

    def transposed_blocks(a):
        return np.ascontiguousarray(a.reshape(blocks, BM, F).transpose(0, 2, 1))

    arrays = {
        "x_rows": np.ascontiguousarray(x.reshape(N // P, P, F).transpose(1, 0, 2)),
        "adj_t": np.ascontiguousarray(adj.reshape(blocks, BM, units, TILES_U, P).transpose(0, 2, 4, 3, 1)),
        "x_t": transposed_blocks(x),
        "h_t": transposed_blocks(h),
    }
    nc = bacc.Bacc("TRN2", target_bir_lowering=False, num_devices=1)
    args = [nc.dram_tensor(name, a.shape, F32, kind="ExternalInput").ap() for name, a in arrays.items()]
    out = nc.dram_tensor("out_t", (blocks, F, BM), F32, kind="ExternalOutput").ap()
    gnn_layer(nc, *args, out)
    r = run_bass_kernel_spmd(nc, [arrays], core_ids=[0])
    return np.ascontiguousarray(r.results[0]["out_t"].transpose(0, 2, 1).reshape(N, F))
```

```python
from contextlib import ExitStack

import concourse.bass as bass
from concourse import mybir

F32 = mybir.dt.float32
F32R = mybir.dt.float32r
ALU = mybir.AluOpType
ACT = mybir.ActivationFunctionType

ALPHA = 0.1
EPS = 1e-05
P = 128
BM = 512
TILES_U = 4
SPLIT = (3, 2)
TILES_G = TILES_U * len(SPLIT)
SPLIT_G = sum(SPLIT)
FIRST = 10
RING = 8
EARLY = 4
SLOTS = 2
HALF = 4096.0
BELOW = 1.0 - 2.0 ** -13


def gnn_layer(nc, adj_t, x_t, h_t, out_t):
    GROUPS, F = x_t.shape[0], x_t.shape[1]
    BLOCKS, UNITS = adj_t.shape[0], adj_t.shape[1]
    KT = GROUPS * TILES_G
    BT = BM // P
    LAPS = UNITS // RING
    assert F == P and UNITS * TILES_U == KT and BLOCKS * BT == KT and UNITS % RING == 0 and UNITS % len(SPLIT) == 0
    PARTS = [SPLIT[u % len(SPLIT)] for u in range(UNITS)]
    PART0 = [sum(PARTS[:u]) for u in range(UNITS)]
    assert FIRST % SLOTS == 0 and BLOCKS % 2 == 0

    def block_of(pair, odd):
        return pair * 2 + (1 if odd else 2)

    def split_units(i, u):
        return i * UNITS + (u - FIRST)

    with ExitStack() as ctx:
        def sb(name, shape, dt=F32):
            return ctx.enter_context(nc.sbuf_tensor(name, shape, dt))

        def sem(name):
            return ctx.enter_context(nc.semaphore(name))

        x_sb = sb("x_sb", [P, KT, P])
        plain_h = sb("plain_h", [P, KT - sum(PARTS), F])
        h1_sb = sb("h1_sb", [P, sum(PARTS), F], F32R)
        h2_sb = sb("h2_sb", [P, sum(PARTS), F], F32R)
        e_sb = sb("e_sb", [P, sum(PARTS), F], F32R)
        adj_sb = sb("adj_sb", [P, RING, TILES_U, BM])
        early_h = sb("early_h", [P, EARLY * SPLIT_G, F])
        a1_sb = sb("a1_sb", [P, SLOTS, max(SPLIT), BM], F32R)
        a2_sb = sb("a2_sb", [P, SLOTS, max(SPLIT), BM], F32R)
        d_sb = sb("d_sb", [P, SLOTS, max(SPLIT), BM], F32R)
        base_sb = sb("base_sb", [P, BM])
        identity = sb("identity", [P, P])
        small_sb = sb("small_sb", [P, BM])
        out_sb = sb("out_sb", [P, BM])
        stats = sb("stats", [P, TILES_G, 6])
        mean2 = sb("mean2", [P, TILES_G])
        shift = sb("shift", [P, TILES_G])
        gap = sb("gap", [P, TILES_G])
        gap2 = sb("gap2", [P, TILES_G])
        spread = sb("spread", [P, TILES_G])
        within = sb("within", [P, TILES_G])
        var = sb("var", [P, TILES_G])
        std = sb("std", [P, TILES_G])
        rough = sb("rough", [P, TILES_G])
        square = sb("square", [P, TILES_G])
        error = sb("error", [P, TILES_G])
        rstd = sb("rstd", [P, TILES_G])
        large = ctx.enter_context(nc.psum_tensor("large", [P, 2, BM], F32))
        small = ctx.enter_context(nc.psum_tensor("small", [P, 2, BM], F32))
        rows = ctx.enter_context(nc.psum_tensor("rows", [P, 2 * TILES_G, F], F32))

        begin_loaded = sem("begin_loaded")
        x_loaded = [sem(f"x_loaded{g}") for g in range(GROUPS)]
        end_loaded = sem("end_loaded")
        adj_loaded = [sem(f"adj_loaded{j}") for j in range(RING)]
        rows_ready = sem("rows_ready")
        cleared = sem("cleared")
        identity_ready = sem("identity_ready")
        base_loaded = sem("base_loaded")
        unit_used = sem("unit_used")
        ln_step = sem("ln_step")
        var_ready = sem("var_ready")
        std_ready = sem("std_ready")
        rstd_ready = sem("rstd_ready")
        scale_ready = sem("scale_ready")
        h_ready = sem("h_ready")
        h1_ready = sem("h1_ready")
        e_ready = sem("e_ready")
        h_split = sem("h_split")
        a1_ready = sem("a1_ready")
        a2_ready = sem("a2_ready")
        d_ready = sem("d_ready")
        a1_free = sem("a1_free")
        small_ready = sem("small_ready")
        small_copied = sem("small_copied")
        large_copied = sem("large_copied")
        base_summed = sem("base_summed")
        partly_summed = sem("partly_summed")
        out_ready = sem("out_ready")
        stored = sem("stored")

        block = ctx.enter_context(nc.Block())

        @block.sync
        def _(sp):
            def load_x(g):
                sp.dma_start(x_sb[:, g * TILES_G:(g + 1) * TILES_G, :], x_t[g]).then_inc(x_loaded[g], 16)

            def load_unit(i, u):
                sp.dma_start(adj_sb[:, u % RING, :, :], adj_t[i, u]).then_inc(adj_loaded[u % RING], 16)

            def load_base(i):
                sp.dma_start(base_sb[:, :], h_t[i]).then_inc(base_loaded, 16)

            x_ahead = {0: [1], 1: [2, 3], 2: [4], 3: [5], 4: [6], 5: [7]}
            half = TILES_G // 2
            sp.dma_start(x_sb[:, 0:half, :], x_t[0, :, 0:half * P]).then_inc(begin_loaded, 16)
            sp.dma_start(x_sb[:, half:TILES_G, :], x_t[0, :, half * P:TILES_G * P]).then_inc(x_loaded[0], 16)
            for u in range(UNITS):
                if u >= RING:
                    sp.wait_ge(unit_used, u - RING + 1)
                load_unit(0, u)
                for g in x_ahead.get(u, []):
                    load_x(g)
            load_base(0)

            def load_block_unit(i, u):
                sp.wait_ge(unit_used, i * UNITS + (u - RING + 1))
                load_unit(i, u)
                if u == RING + 4:
                    sp.wait_ge(out_ready, i)
                    load_base(i)

            with sp.Fori(1, BLOCKS - 1) as i:
                for u in range(UNITS):
                    load_block_unit(i, u)
            for u in range(UNITS - 1):
                load_block_unit(BLOCKS - 1, u)
            sp.wait_ge(unit_used, BLOCKS * UNITS - RING)
            half = TILES_U // 2
            for at, loaded in ((0, adj_loaded[(UNITS - 1) % RING]), (half, end_loaded)):
                sp.dma_start(adj_sb[:, (UNITS - 1) % RING, at:at + half, :],
                             adj_t[BLOCKS - 1, UNITS - 1, :, at:at + half, :]).then_inc(loaded, 16)

        @block.gpsimd
        def _(pool):
            nc.gpsimd.memset(identity[:, :], 0.0).then_inc(cleared, 1)
            pool.wait_ge(cleared, 1)
            nc.gpsimd.affine_select(out=identity[:, :], in_=identity[:, :], compare_op=ALU.not_equal, fill=1.0,
                                    base=0, pattern=[[-1, P]], channel_multiplier=1).then_inc(identity_ready, 1)
            for g in range(GROUPS):
                pool.wait_ge(e_ready, g + 1)
                part = e_sb[:, g * SPLIT_G:(g + 1) * SPLIT_G, :]
                nc.gpsimd.tensor_scalar(part, part.bitcast(F32), HALF, 1.0, ALU.mult, ALU.mult).then_inc(h_split, 1)

        @block.tensor
        def _(pe):
            def turn(g):
                pe.wait_ge(begin_loaded if g == 0 else x_loaded[g], 16)
                if g >= 2:
                    pe.wait_ge(h_ready, (g - 1) * TILES_G)
                for k in range(TILES_G):
                    if g == 0 and k == TILES_G // 2:
                        pe.wait_ge(x_loaded[0], 16)
                    mm = nc.tensor.transpose(rows[:, g % 2 * TILES_G + k, :], x_sb[:, g * TILES_G + k, :],
                                             identity[:, :])
                    if k % BT == BT - 1:
                        mm.then_inc(rows_ready, 1)

            def stationary(u, k):
                if k >= PARTS[u]:
                    return plain_h[:, u * TILES_U - PART0[u] + k - PARTS[u], :]
                return early_h[:, PART0[u] % (EARLY * SPLIT_G) + k, :]

            def small_products(i, odd, u, first, last):
                s, n, count = u % SLOTS, PARTS[u], split_units(i, u) + 1
                pe.wait_ge(a1_ready, count)
                for k in range(n):
                    nc.tensor.matmul(small[:, odd, :], h1_sb[:, PART0[u] + k, :], a1_sb[:, s, k, :],
                                     start=(first and k == 0), stop=False)
                pe.wait_ge(a2_ready, count)
                for k in range(n):
                    mm = nc.tensor.matmul(small[:, odd, :], h2_sb[:, PART0[u] + k, :], a2_sb[:, s, k, :],
                                          start=False, stop=(last and k == n - 1))
                if last:
                    mm.then_inc(small_ready, 1)

            def large_products(i, odd, u, last):
                s, n, count = u % SLOTS, PARTS[u], split_units(i, u) + 1
                pe.wait_ge(d_ready, count)
                for k in range(n):
                    mm = nc.tensor.matmul(large[:, odd, :], e_sb[:, PART0[u] + k, :], d_sb[:, s, k, :],
                                          start=False, stop=(last and k == n - 1))
                    if k == 0:
                        mm.then_inc(a1_free, 1)
                mm.then_inc(unit_used, 1)

            def plain_products(odd, u, k0, k1=TILES_U):
                for k in range(k0, k1):
                    mm = nc.tensor.matmul(large[:, odd, :], stationary(u, k), adj_sb[:, u % RING, k, :],
                                          start=(u == 0 and k == k0), stop=False)
                return mm

            def mixed_unit(i, odd, u, first, last):
                pe.wait_ge(adj_loaded[u % RING], i * (16 * LAPS) + 16 * (u // RING + 1))
                plain_products(odd, u, PARTS[u])
                small_products(i, odd, u, first, last)
                large_products(i, odd, u, last)

            pe.wait_ge(identity_ready, 1)
            turn(0)
            turn(1)
            for u in range(UNITS):
                if 2 <= u + 1 < GROUPS:
                    turn(u + 1)
                if u < FIRST:
                    pe.wait_ge(adj_loaded[u % RING], 16 * (u // RING + 1))
                    for k in range(TILES_U):
                        pe.wait_ge(h_ready, u * TILES_U + k + 1)
                        mm = nc.tensor.matmul(large[:, 0, :], stationary(u, k), adj_sb[:, u % RING, k, :],
                                              start=(u == 0 and k == 0), stop=False)
                    mm.then_inc(unit_used, 1)
                else:
                    if u % len(SPLIT) == 0:
                        pe.wait_ge(h_split, u // len(SPLIT) + 1)
                    mixed_unit(0, 0, u, u == FIRST, u == UNITS - 1)
            with pe.Fori(0, BLOCKS // 2 - 1) as pair:
                for odd in (1, 0):
                    i = block_of(pair, odd)
                    for u in range(UNITS):
                        mixed_unit(i, odd, u, u == 0, u == UNITS - 1)
                    pe.wait_ge(small_copied, i)
                    pe.wait_ge(large_copied, i)
            for u in range(UNITS - 2):
                mixed_unit(BLOCKS - 1, 1, u, u == 0, False)
            i, u = BLOCKS - 1, UNITS - 1
            for j in (u - 1, u):
                pe.wait_ge(adj_loaded[j % RING], i * (16 * LAPS) + 16 * (j // RING + 1))
                plain_products(1, j, PARTS[j] if j < u else 0, TILES_U if j < u else TILES_U // 2)
            small_products(i, 1, u - 1, False, True)
            pe.wait_ge(end_loaded, 16)
            plain_products(1, u, TILES_U // 2).then_inc(unit_used, 1)
            large_products(i, 1, u - 1, True)

        @block.scalar
        def _(act):
            def deviation(g):
                act.wait_ge(var_ready, g + 1)
                nc.scalar.activation(std[:, :], var[:, :], ACT.Sqrt).then_inc(std_ready, 1)

            def normalise(g):
                act.wait_ge(scale_ready, g + 1)
                for k in range(TILES_G):
                    j, t = k // TILES_U, k % TILES_U
                    if t < SPLIT[j]:
                        tile = early_h[:, bass.ds(g % EARLY * SPLIT_G + sum(SPLIT[:j]) + t, 1), :]
                    else:
                        at = j * TILES_U - sum(SPLIT[:j + 1]) + t
                        tile = plain_h[:, bass.ds(g * (TILES_G - SPLIT_G) + at, 1), :]
                    nc.scalar.activation(tile, rows[:, bass.ds(g % 2 * TILES_G + k, 1), :], ACT.Relu,
                                         scale=rstd[:, k:k + 1], bias=shift[:, k:k + 1]).then_inc(h_ready, 1)

            def leading_h(g):
                act.wait_ge(h_ready, g * TILES_G + TILES_G)
                nc.scalar.activation(h1_sb[:, bass.ds(g * SPLIT_G, SPLIT_G), :],
                                     early_h[:, bass.ds(g % EARLY * SPLIT_G, SPLIT_G), :], ACT.Copy,
                                     scale=BELOW / HALF).then_inc(h1_ready, 1)

            deviation(0)
            normalise(0)
            with act.Fori(1, EARLY) as g:
                deviation(g)
                leading_h(g - 1)
                normalise(g)
            with act.Fori(EARLY, GROUPS) as g:
                deviation(g)
                leading_h(g - 1)
                act.wait_ge(unit_used, (g - EARLY + 1) * len(SPLIT))
                normalise(g)
            leading_h(GROUPS - 1)

            def copy_small(i, odd):
                act.wait_ge(small_ready, i)
                nc.scalar.activation(small_sb[:, :], small[:, odd, :], ACT.Copy,
                                     scale=(1.0 - ALPHA) * (HALF + 1.0)).then_inc(small_copied, 1)

            def copy_large(i, odd):
                act.wait_ge(unit_used, i * UNITS)
                nc.scalar.activation(out_sb[:, :], large[:, odd, :], ACT.Copy,
                                     scale=1.0 - ALPHA).then_inc(large_copied, 1)

            def store(i):
                act.wait_ge(out_ready, i)
                act.dma_start(out_t[i - 1], out_sb[:, :]).then_inc(stored, 16)

            def leading_part(i, u):
                s, n = u % SLOTS, PARTS[u]
                act.wait_ge(adj_loaded[u % RING], i * (16 * LAPS) + 16 * (u // RING + 1))
                act.wait_ge(a1_free, split_units(i, u) + 1)
                nc.scalar.activation(a1_sb[:, s, 0:n, :], adj_sb[:, u % RING, 0:n, :],
                                     ACT.Copy, scale=BELOW).then_inc(a1_ready, 1)

            def rest(i, odd, u):
                if u == 1:
                    copy_small(i, 1 - odd)
                    copy_large(i, 1 - odd)
                if u == 8:
                    store(i)
                if u == UNITS - 1:
                    act.wait_ge(stored, i * 16)

            for u in range(FIRST, UNITS):
                leading_part(0, u)
            with act.Fori(0, BLOCKS // 2 - 1) as pair:
                for odd in (1, 0):
                    i = block_of(pair, odd)
                    for u in range(UNITS):
                        leading_part(i, u)
                        rest(i, odd, u)
            for u in range(UNITS):
                if u < UNITS - 1:
                    leading_part(BLOCKS - 1, u)
                rest(BLOCKS - 1, 1, u)
            copy_small(BLOCKS, 1)
            store(BLOCKS)
            act.wait_ge(stored, 16 * BLOCKS)

        @block.vector
        def _(dve):
            dve.sem_inc(a1_free, SLOTS)

            def normalisation(g):
                STEPS = 6
                for k in range(TILES_G):
                    if k % BT == 0:
                        dve.wait_ge(rows_ready, g * (TILES_G // BT) + (k // BT + 1))
                    last = nc.vector.bn_stats(stats[:, k, :], rows[:, bass.ds(g % 2 * TILES_G + k, 1), :])
                last.then_inc(ln_step, 1)
                dve.wait_ge(ln_step, g * STEPS + 1)
                nc.vector.tensor_tensor(gap[:, :], stats[:, :, 1], stats[:, :, 4], ALU.subtract)
                nc.vector.tensor_tensor(spread[:, :], stats[:, :, 2], stats[:, :, 5], ALU.add)
                nc.vector.tensor_tensor(mean2[:, :], stats[:, :, 1], stats[:, :, 4],
                                        ALU.add).then_inc(ln_step, 1)
                dve.wait_ge(ln_step, g * STEPS + 2)
                nc.vector.tensor_scalar(within[:, :], spread[:, :], 1.0 / F, EPS, ALU.mult, ALU.add)
                nc.vector.scalar_tensor_tensor(gap2[:, :], gap[:, :], 0.25, gap[:, :],
                                               ALU.mult, ALU.mult).then_inc(ln_step, 1)
                dve.wait_ge(ln_step, g * STEPS + 3)
                nc.vector.tensor_tensor(var[:, :], within[:, :], gap2[:, :], ALU.add).then_inc(var_ready, 1)
                dve.wait_ge(std_ready, g + 1)
                nc.vector.reciprocal(rough[:, :], std[:, :]).then_inc(ln_step, 1)
                dve.wait_ge(ln_step, g * STEPS + 4)
                nc.vector.tensor_tensor(square[:, :], rough[:, :], rough[:, :], ALU.mult).then_inc(ln_step, 1)
                dve.wait_ge(ln_step, g * STEPS + 5)
                nc.vector.scalar_tensor_tensor(error[:, :], square[:, :], -0.5, var[:, :],
                                               ALU.mult, ALU.mult).then_inc(ln_step, 1)
                dve.wait_ge(ln_step, g * STEPS + 6)
                if not isinstance(g, int):
                    dve.wait_ge(h_ready, g * TILES_G)
                nc.vector.scalar_tensor_tensor(rstd[:, :], error[:, :], 1.5, rough[:, :],
                                               ALU.add, ALU.mult).then_inc(rstd_ready, 1)
                dve.wait_ge(rstd_ready, g + 1)
                nc.vector.scalar_tensor_tensor(shift[:, :], mean2[:, :], -0.5, rstd[:, :],
                                               ALU.mult, ALU.mult).then_inc(scale_ready, 1)

            def trailing_h(g):
                dve.wait_ge(h1_ready, g + 1)
                part = bass.ds(g * SPLIT_G, SPLIT_G)
                h1 = h1_sb[:, part, :].bitcast(F32)
                h = early_h[:, bass.ds(g % EARLY * SPLIT_G, SPLIT_G), :]
                nc.vector.scalar_tensor_tensor(h2_sb[:, part, :], h1, -HALF, h, ALU.mult, ALU.add)
                nc.vector.scalar_tensor_tensor(e_sb[:, part, :], h1, -(HALF + 1.0), h,
                                               ALU.mult, ALU.add).then_inc(e_ready, 1)

            normalisation(0)
            with dve.Fori(1, GROUPS) as g:
                normalisation(g)
                trailing_h(g - 1)
            trailing_h(GROUPS - 1)

            def base(i):
                dve.wait_ge(base_loaded, i * 16 + 16)
                nc.vector.scalar_tensor_tensor(base_sb[:, :], base_sb[:, :], ALPHA, x_sb[:, bass.ds(i * BT, BT), :],
                                               ALU.mult, ALU.add).then_inc(base_summed, 1)

            def finish(i, at_end=False):
                dve.wait_ge(base_summed, i)
                dve.wait_ge(small_copied, i)
                nc.vector.tensor_tensor(base_sb[:, :], base_sb[:, :], small_sb[:, :],
                                        ALU.add).then_inc(partly_summed, 1)
                dve.wait_ge(partly_summed, i)
                if at_end:
                    dve.wait_ge(unit_used, BLOCKS * UNITS)
                    nc.vector.scalar_tensor_tensor(out_sb[:, :], large[:, 1, :], 1.0 - ALPHA, base_sb[:, :],
                                                   ALU.mult, ALU.add).then_inc(out_ready, 1)
                    return
                dve.wait_ge(large_copied, i)
                nc.vector.tensor_tensor(out_sb[:, :], out_sb[:, :], base_sb[:, :],
                                        ALU.add).then_inc(out_ready, 1)

            def trailing_parts(i, u):
                s, n, count = u % SLOTS, PARTS[u], split_units(i, u) + 1
                a = adj_sb[:, u % RING, 0:n, :]
                a1 = a1_sb[:, s, 0:n, :].bitcast(F32)
                dve.wait_ge(a1_ready, count)
                if not (isinstance(i, int) and i == 0 and u < FIRST + SLOTS):
                    dve.wait_ge(unit_used, i * UNITS + (u - SLOTS + 1))
                nc.vector.tensor_tensor(a2_sb[:, s, 0:n, :], a, a1, ALU.subtract).then_inc(a2_ready, 1)
                nc.vector.scalar_tensor_tensor(d_sb[:, s, 0:n, :], a1, 1.0 + 1.0 / HALF, a,
                                               ALU.mult, ALU.subtract).then_inc(d_ready, 1)

            for u in range(FIRST, UNITS):
                trailing_parts(0, u)
            base(0)
            with dve.Fori(1, BLOCKS - 1) as i:
                for u in range(UNITS):
                    trailing_parts(i, u)
                    if u == 2:
                        finish(i)
                    if u == 12:
                        base(i)
            for u in range(UNITS - 1):
                trailing_parts(BLOCKS - 1, u)
                if u == 2:
                    finish(BLOCKS - 1)
                if u == 12:
                    base(BLOCKS - 1)
            finish(BLOCKS, at_end=True)


def kernel(x, adj, L0_gnn_h):
    import numpy as np
    import concourse.bacc as bacc
    from concourse.bass_utils import run_bass_kernel_spmd

    x, adj, h = (np.asarray(a) for a in (x, adj, L0_gnn_h))
    N, F = x.shape
    blocks, units = N // BM, N // (P * TILES_U)

    def transposed(a, rows):
        return np.ascontiguousarray(a.reshape(-1, rows, F).transpose(0, 2, 1))

    arrays = {
        "adj_t": np.ascontiguousarray(adj.reshape(blocks, BM, units, TILES_U, P).transpose(0, 2, 4, 3, 1)),
        "x_t": transposed(x, TILES_G * P),
        "h_t": transposed(h, BM),
    }
    nc = bacc.Bacc("TRN2", target_bir_lowering=False, num_devices=1,
                   dynamic_dma_scratch_size=1024)
    args = [nc.dram_tensor(name, a.shape, F32, kind="ExternalInput").ap() for name, a in arrays.items()]
    out = nc.dram_tensor("out_t", (blocks, F, BM), F32, kind="ExternalOutput").ap()
    gnn_layer(nc, *args, out)
    r = run_bass_kernel_spmd(nc, [arrays], core_ids=[0])
    return np.ascontiguousarray(r.results[0]["out_t"].transpose(0, 2, 1).reshape(N, F))
```
